# Optimizing a Trainium2 kernel written in Bass

```python
import numpy as np
import jax
import jax.numpy as jnp

def _softmax(x, axis=-1):
    return jax.nn.softmax(x, axis=axis)

def _gelu(x):
    return jax.nn.gelu(x, approximate=True)

def _silu(x):
    return jax.nn.silu(x)

def _sigmoid(x):
    return jax.nn.sigmoid(x)

def _layernorm(x, axis=-1, eps=1e-05):
    m = jnp.mean(x, axis=axis, keepdims=True)
    v = jnp.var(x, axis=axis, keepdims=True)
    return (x - m) / jnp.sqrt(v + eps)

def _scatter_add(tgt, idx, src, axis=0):
    return tgt.at[idx].add(src)

def _segment_sum(src, seg, n):
    return jax.ops.segment_sum(src, seg, n)
kernel_name = 'mk_adj_resnorm_d4_adj_r2_22e05a'

def setup_inputs(seed: int=0):
    np.random.seed(seed)
    _w = jnp.asarray

    def _rec_inputs():
        import jax
        import jax.numpy as jnp
        _gk = jax.random.key(seed)
        x = -0.0005207 + 1.001 * jax.random.normal(jax.random.fold_in(_gk, 1), (4096, 128), jnp.float32)
        _w = (1.0 + jnp.arange(4096, dtype=jnp.float32)) ** (-0.5)
        _w = _w / _w.mean()
        _pij = jnp.clip(0.000976562 * _w[:, None] * _w[None, :], 0.0, 1.0)
        _a = jax.random.uniform(jax.random.fold_in(_gk, 2), (4096, 4096)) < _pij
        _a = jnp.logical_or(_a, jnp.eye(4096, dtype=bool))
        _af = _a.astype(jnp.float32)
        _af = _af * jax.random.uniform(jax.random.fold_in(_gk, 3), (4096, 4096), jnp.float32, 0.05, 1)
        adj = _af
        return (x, adj)
    x, adj = _rec_inputs()

    def _L0_gnn_setup():
        import jax, jax.numpy as jnp
        import numpy as np
        key = jax.random.key(seed)
        k1, k2, k3, k4 = jax.random.split(key, 4)
        n, in_dim, out_dim = (8192, 128, 128)
        h = jax.random.normal(k1, (n, in_dim), dtype=jnp.float32)
        adj = jax.random.uniform(k2, (n, n), dtype=jnp.float32)
        W_self = jax.random.normal(k3, (in_dim, out_dim), dtype=jnp.float32) * (1.0 / np.sqrt(in_dim))
        W_neigh = jax.random.normal(k4, (in_dim, out_dim), dtype=jnp.float32) * (1.0 / np.sqrt(in_dim))
        return {'h': h, 'adj': adj, 'W_self': W_self, 'W_neigh': W_neigh}
    _L0_gnn_all = _L0_gnn_setup()
    _L0_gnn_in = {k: v for k, v in _L0_gnn_all.items() if k in ('W_self', 'W_neigh')}
    del _L0_gnn_all

    def _L1_gnn_setup():
        import jax, jax.numpy as jnp
        import numpy as np
        N = 8192
        F_IN = 128
        F_OUT = 128
        key = jax.random.key(seed)
        k1, k2, k3, k4 = jax.random.split(key, 4)
        features = jax.random.normal(k1, (N, F_IN), dtype=jnp.float32)
        adj = jax.random.uniform(k2, (N, N), dtype=jnp.float32)
        kernel = jax.random.normal(k3, (F_IN, F_OUT), dtype=jnp.float32) * 0.02
        bias = jax.random.normal(k4, (F_OUT,), dtype=jnp.float32) * 0.02
        return {'features': features, 'adj': adj, 'kernel': kernel, 'bias': bias}
    _L1_gnn_all = _L1_gnn_setup()
    _L1_gnn_in = {k: v for k, v in _L1_gnn_all.items() if k in ('kernel', 'bias')}
    del _L1_gnn_all

    def _L2_gnn_setup():
        import jax, jax.numpy as jnp
        import numpy as np
        N = 4096
        D = 128
        key = jax.random.key(seed)
        kx, ka, kw1, kw2 = jax.random.split(key, 4)
        x = jax.random.normal(kx, (N, D), dtype=jnp.float32)
        A = jax.random.uniform(ka, (N, N), dtype=jnp.float32)
        s = 0.05
        W1 = jax.random.normal(kw1, (D, D), dtype=jnp.float32) * s
        b1 = jnp.zeros((D,), dtype=jnp.float32)
        W2 = jax.random.normal(kw2, (D, D), dtype=jnp.float32) * s
        b2 = jnp.zeros((D,), dtype=jnp.float32)
        return {'x': x, 'A': A, 'W1': W1, 'b1': b1, 'W2': W2, 'b2': b2}
    _L2_gnn_all = _L2_gnn_setup()
    _L2_gnn_in = {k: v for k, v in _L2_gnn_all.items() if k in ('W1', 'b1', 'W2', 'b2')}
    del _L2_gnn_all

    def _L3_gnn_setup():
        import jax, jax.numpy as jnp
        import numpy as np
        N = 8192
        U = 128
        AVG_DEGREE = 32
        key = jax.random.key(seed)
        kx, ka, kw = jax.random.split(key, 3)
        x = jax.random.normal(kx, (N, U), dtype=jnp.float32)
        adj = (jax.random.uniform(ka, (N, N)) < AVG_DEGREE / N).astype(jnp.float32)
        W = jax.random.normal(kw, (U, U), dtype=jnp.float32) * 0.05
        b = jnp.zeros((U,), dtype=jnp.float32)
        return {'x': x, 'adj': adj, 'W': W, 'b': b}
    _L3_gnn_all = _L3_gnn_setup()
    _L3_gnn_in = {k: v for k, v in _L3_gnn_all.items() if k in ('W', 'b')}
    del _L3_gnn_all
    return {'x': x, 'adj': adj, 'L0_gnn_W_self': _L0_gnn_in['W_self'], 'L0_gnn_W_neigh': _L0_gnn_in['W_neigh'], 'L1_gnn_kernel': _L1_gnn_in['kernel'], 'L1_gnn_bias': _L1_gnn_in['bias'], 'L2_gnn_W1': _L2_gnn_in['W1'], 'L2_gnn_b1': _L2_gnn_in['b1'], 'L2_gnn_W2': _L2_gnn_in['W2'], 'L2_gnn_b2': _L2_gnn_in['b2'], 'L3_gnn_W': _L3_gnn_in['W'], 'L3_gnn_b': _L3_gnn_in['b']}

def reference(x, adj, L0_gnn_W_self, L0_gnn_W_neigh, L1_gnn_kernel, L1_gnn_bias, L2_gnn_W1, L2_gnn_b1, L2_gnn_W2, L2_gnn_b2, L3_gnn_W, L3_gnn_b):
    import jax
    import jax.numpy as jnp

    def _L0_gnn_ref(h, adj, W_self, W_neigh):
        import jax, jax.numpy as jnp
        import numpy as np
        deg = jnp.clip(jnp.sum(adj, axis=1, keepdims=True), 1.0)
        h_neigh = adj @ h / deg
        return h @ W_self + h_neigh @ W_neigh

    def _L1_gnn_ref(features, adj, kernel, bias):
        import jax, jax.numpy as jnp
        import numpy as np
        N = 8192
        F_IN = 128
        F_OUT = 128
        xw = features @ kernel
        out = adj @ xw
        return jax.nn.relu(out + bias)

    def _L2_gnn_ref(x, A, W1, b1, W2, b2):
        import jax, jax.numpy as jnp
        import numpy as np
        N = 4096
        D = 128
        h = jax.nn.relu(jnp.matmul(A, jnp.matmul(x, W1)) + b1)
        h = jax.nn.relu(jnp.matmul(A, jnp.matmul(h, W2)) + b2)
        return h

    def _L3_gnn_ref(x, adj, W, b):
        import jax, jax.numpy as jnp
        import numpy as np
        N = 8192
        U = 128
        AVG_DEGREE = 32
        adj = jax.lax.stop_gradient(adj)
        neigh1 = adj @ x
        x1 = jax.nn.swish(neigh1 @ W + b)
        neigh2 = adj @ x1
        x2 = jax.nn.swish(neigh2 @ W + b)
        return x2
    x = _layernorm(x + _L0_gnn_ref(x, adj, L0_gnn_W_self, L0_gnn_W_neigh), axis=-1)
    x = _layernorm(x + _L1_gnn_ref(x, adj, L1_gnn_kernel, L1_gnn_bias), axis=-1)
    x = _layernorm(x + _L2_gnn_ref(x, adj, L2_gnn_W1, L2_gnn_b1, L2_gnn_W2, L2_gnn_b2), axis=-1)
    x = _layernorm(x + _L3_gnn_ref(x, adj, L3_gnn_W, L3_gnn_b), axis=-1)
    return x

_drawn_inputs = setup_inputs


def setup_inputs(seed=0):
    import zlib

    import numpy as np

    out = dict(_drawn_inputs(seed))
    spreads = {'L2_gnn_b1': (0.0, 0.1), 'L2_gnn_b2': (0.0, 0.1), 'L3_gnn_b': (0.0, 0.1)}
    factors = {}
    for name, (base, spread) in spreads.items():
        noise = np.random.default_rng([zlib.crc32(name.encode()), seed]).standard_normal(out[name].shape)
        drawn = base * np.exp(spread * noise) if base else spread * noise
        out[name] = jnp.asarray(drawn.astype(out[name].dtype))
    for name, factor in factors.items():
        out[name] = (out[name] * factor).astype(out[name].dtype)
    return out
```

```python
import concourse.bass as bass
from concourse import mybir
from contextlib import ExitStack


def bass_gnn_residual_norm_kernel(
    nc: bass.Bass,
    adj_tiles: bass.AP,
    x_blocks: bass.AP,
    x_t: bass.AP,
    W_self: bass.AP,
    W_neigh: bass.AP,
    L1_kernel: bass.AP,
    L1_bias: bass.AP,
    W1: bass.AP,
    b1: bass.AP,
    W2: bass.AP,
    b2: bass.AP,
    L3_W: bass.AP,
    L3_b: bass.AP,
    out: bass.AP,
):
    fp32 = mybir.dt.float32
    fp32r = mybir.dt.float32r
    ALU = mybir.AluOpType
    ACT = mybir.ActivationFunctionType
    P = 128

    D = x_t.shape[0]
    N = x_t.shape[1]
    CHUNKS, TILES = adj_tiles.shape[0], adj_tiles.shape[1]
    NB = N // P
    CW = N // CHUNKS
    BPT = NB // TILES
    TW = BPT * CW
    BPC = CW // P
    GW = BPT * D
    PASSES = 6
    SLOTS = 7
    STREAMED = 2 * SLOTS
    KEPT = TILES - STREAMED
    LOADS = STREAMED // SLOTS
    SPLITS = 4
    X_PARTS = 4
    EPS = 1e-5
    NORM_PASSES = [0, 1, 3]
    RELU_PASSES = [1, 3]
    HIDDEN_PASSES = [2, 4]
    LAST = PASSES - 1

    ctx = ExitStack()
    with ctx:
        def sb(name, shape, dt=fp32):
            return ctx.enter_context(nc.sbuf_tensor(name, shape, dt))

        def pb(name, shape):
            return ctx.enter_context(nc.psum_tensor(name, shape, fp32))

        def sem(name):
            return ctx.enter_context(nc.semaphore(name))

        xT = sb("xT", [P, N])
        hidden = sb("hidden", [P, N])
        op_hi = sb("op_hi", [P, N], fp32r)
        op_lo = sb("op_lo", [P, N], fp32r)
        kept = sb("kept", [P, CHUNKS * KEPT, TW])   
        ring = sb("ring", [P, SLOTS, TW])
        adj_hi = sb("adj_hi", [P, SPLITS, TW], fp32r)
        adj_lo = sb("adj_lo", [P, SPLITS, TW], fp32r)
        w_self = sb("w_self", [P, D])
        w_neigh = sb("w_neigh", [P, D])
        w_l1 = sb("w_l1", [P, D])
        w_1 = sb("w_1", [P, D])
        w_2 = sb("w_2", [P, D])
        w_3 = sb("w_3", [P, D])
        b3_rows = sb("b3_rows", [P, D])
        bias_l1 = sb("bias_l1", [P, 1])
        bias_1 = sb("bias_1", [P, 1])
        bias_2 = sb("bias_2", [P, 1])
        eps = sb("eps", [P, 1])
        ident = sb("ident", [P, P])
        center = sb("center", [P, P])
        mean_of = sb("mean_of", [P, P])
        deg_part = sb("deg_part", [P, TW])
        deg_sum = sb("deg_sum", [P, CW])
        t_in = sb("t_in", [P, CW])
        t_y = sb("t_y", [P, CW])
        t_sq = sb("t_sq", [P, CW])
        t_std = sb("t_std", [P, CW])
        stats = sb("stats", [P, BPC, 6])
        mean_even = sb("mean_even", [P, BPC])
        moments = sb("moments", [P, BPC, 2])
        var_eps = sb("var_eps", [P, BPC])
        rstd = sb("rstd", [P, BPC])
        minus_half = sb("minus_half", [P, BPC])

        WEIGHTS = [(w_self[:], W_self), (w_neigh[:], W_neigh), (w_l1[:], L1_kernel), (w_1[:], W1), (w_2[:], W2),
                   (w_3[:], L3_W), (bias_l1[:], L1_bias), (bias_1[:], b1), (bias_2[:], b2),
                   (b3_rows[:], L3_b.partition_broadcast(P))]

        agg = pb("agg", [P, 2 * CW])
        p_gen = pb("p_gen", [P, 2, 512])
        p_deg = pb("p_deg", [P, CW])
        p_mix = pb("p_mix", [P, CW])
        p_cen = pb("p_cen", [P, CW])
        p_var = pb("p_var", [P, CW])

        x_loaded = [sem(f"x_loaded{i}") for i in range(X_PARTS)]
        xt_loaded = sem("xt_loaded")
        w_loaded = sem("w_loaded")
        slot_loaded = [sem(f"slot_loaded{s}") for s in range(SLOTS)]
        kept_loaded = sem("kept_loaded")
        ident_zeroed = sem("ident_zeroed")
        ident_ready = sem("ident_ready")
        consts_ready = sem("consts_ready")
        center_ready = sem("center_ready")
        tile_used = sem("tile_used")
        vec_tile = sem("vec_tile")
        hi_ready = sem("hi_ready")
        deg_ready = sem("deg_ready")
        deg_done = sem("deg_done")
        deg_step = sem("deg_step")
        neigh_ready = sem("neigh_ready")
        mix_done = sem("mix_done")
        relu_ready = sem("relu_ready")
        y_ready = sem("y_ready")
        cen_done = sem("cen_done")
        sq_ready = sem("sq_ready")
        var_done = sem("var_done")
        std_ready = sem("std_ready")
        inv_ready = sem("inv_ready")
        x_ready = sem("x_ready")
        hidden_ready = sem("hidden_ready")
        gen_done = sem("gen_done")
        zb_ready = sem("zb_ready")
        swish_ready = sem("swish_ready")
        gen_hi = sem("gen_hi")
        gen_lo = sem("gen_lo")
        last_in = sem("last_in")
        last_z = sem("last_z")
        last_zb = sem("last_zb")
        last_act = sem("last_act")
        last_y = sem("last_y")
        last_stats = sem("last_stats")
        last_moments = sem("last_moments")
        last_var = sem("last_var")
        last_rstd = sem("last_rstd")
        last_out = sem("last_out")
        stored = sem("stored")

        block = ctx.enter_context(nc.Block())

        def nth(passes, p, c):
            return passes.index(p) * CHUNKS + c

        def chunk_of(t, c):
            return t[:, bass.ds(c * CW, CW)]

        def bank_of(c):
            return agg[:, bass.ds((c % 2) * CW, CW)]

        def raw_tile(c, t):
            if t < STREAMED:
                return ring[:, t % SLOTS, :]
            return kept[:, bass.ds(c * KEPT + t - STREAMED, 1), :].rearrange("p o n -> p (o n)")

        def op_tile(buf, t):
            return buf[:, t * GW:(t + 1) * GW]

        def wait_loaded(eng, p, c, t):
            if t < STREAMED:
                eng.wait_ge(slot_loaded[t % SLOTS], 16 * (LOADS * (p * CHUNKS + c) + t // SLOTS + 1))
            elif t == STREAMED and p == 0:
                eng.wait_ge(kept_loaded, 16 * (c + 1))

        @block.sync
        def _(sp):
            def load_chunk(p, c):
                first = isinstance(c, int)
                for t in range(STREAMED):
                    before = (p * CHUNKS + c) * TILES + t + 1 - SLOTS - (KEPT if t < SLOTS else 0)
                    if not (p == 0 and first and t < SLOTS):
                        if p == 0 or (p == 1 and first and t < SLOTS):
                            sp.wait_ge(tile_used, before)
                        sp.wait_ge(vec_tile, before)
                    sp.dma_start(ring[:, t % SLOTS, :], adj_tiles[c, t]).then_inc(slot_loaded[t % SLOTS], 16)
                if p == 0:
                    if not first:
                        sp.wait_ge(kept_loaded, 16 * c)
                    sp.dma_start(kept[:, bass.ds(c * KEPT, KEPT), :],
                                 adj_tiles[c, STREAMED:TILES].rearrange("t p n -> p t n")).then_inc(kept_loaded, 16)

            for p in range(PASSES):
                load_chunk(p, 0)
                with sp.Fori(1, CHUNKS) as c:
                    load_chunk(p, c)

        @block.tensor
        def _(pe):
            def gen(p, t):
                c_of = t * BPT // BPC
                if p in (1, 2, 4):
                    src = xT
                    pe.wait_ge(x_ready, nth(NORM_PASSES, {1: 0, 2: 1, 4: 3}[p], c_of) + 1)
                else:
                    src = hidden
                    pe.wait_ge(hidden_ready, nth(HIDDEN_PASSES, p - 1, c_of) + 1)
                for b in range(BPT):
                    j = t * BPT + b
                    dst = p_gen[:, t % 2, b * D:(b + 1) * D]
                    if p == 4:
                        last = nc.tensor.transpose(dst, src[:, j * P:(j + 1) * P], ident[:])
                    else:
                        w = {1: w_l1, 2: w_1, 3: w_2, 5: w_3}[p]
                        last = nc.tensor.matmul(dst, src[:, j * P:(j + 1) * P], w[:], start=True, stop=True)
                last.then_inc(gen_done, 1)

            def tile_whole(c, t):
                wait_loaded(pe, 0, c, t)
                raw = raw_tile(c, t)
                for b in range(BPT):
                    j = t * BPT + b
                    last = nc.tensor.matmul(bank_of(c), hidden[:, j * D:(j + 1) * D],
                                            raw[:, b * CW:(b + 1) * CW], start=(j == 0), stop=(j == NB - 1))
                last.then_inc(tile_used, 1)

            def tile_split(p, c, t):
                s = t % SPLITS
                pe.wait_ge(hi_ready, ((p - 1) * CHUNKS + c) * TILES + t + 1)
                for b in range(BPT):
                    j = t * BPT + b
                    a_hi = adj_hi[:, s, b * CW:(b + 1) * CW]
                    nc.tensor.matmul(bank_of(c), op_hi[:, j * D:(j + 1) * D], a_hi, start=(j == 0), stop=False)
                    nc.tensor.matmul(bank_of(c), op_lo[:, j * D:(j + 1) * D], a_hi, start=False, stop=False)
                pe.wait_ge(vec_tile, (p * CHUNKS + c) * TILES + t + 1)
                for b in range(BPT):
                    j = t * BPT + b
                    last = nc.tensor.matmul(bank_of(c), op_hi[:, j * D:(j + 1) * D],
                                            adj_lo[:, s, b * CW:(b + 1) * CW], start=False, stop=(j == NB - 1))
                last.then_inc(tile_used, 1)

            def post(p, c, at):
                if p == 0 and at == 0:
                    pe.wait_ge(deg_ready, c + 1)
                    nc.tensor.matmul(p_deg[:], mean_of[:], deg_sum[:], start=True, stop=True).then_inc(deg_done, 1)
                if p == 0 and at == 3:
                    pe.wait_ge(neigh_ready, c + 1)
                    nc.tensor.matmul(p_mix[:], w_self[:], chunk_of(xT, c), start=True, stop=False)
                    nc.tensor.matmul(p_mix[:], w_neigh[:], t_in[:], start=False, stop=True).then_inc(mix_done, 1)
                if p in NORM_PASSES:
                    n = nth(NORM_PASSES, p, c)
                    if at == (6 if p == 0 else 1):
                        pe.wait_ge(y_ready, n + 1)
                        nc.tensor.matmul(p_cen[:], center[:], t_y[:], start=True, stop=True).then_inc(cen_done, 1)
                    if at == (8 if p == 0 else 3):
                        pe.wait_ge(sq_ready, n + 1)
                        nc.tensor.matmul(p_var[:], mean_of[:], t_sq[:], start=True, stop=True).then_inc(var_done, 1)
                if p in HIDDEN_PASSES and at == 6:
                    pe.wait_ge(hidden_ready, nth(HIDDEN_PASSES, p, c) + 1)
                if p == LAST and at == 1:
                    pe.wait_ge(last_in, 2 * (c + 1))
                    for b in range(BPC):
                        nc.tensor.matmul(p_mix[:, b * D:(b + 1) * D], t_in[:, b * P:(b + 1) * P], w_3[:],
                                         start=True, stop=True)
                    for b in range(BPC):
                        last = nc.tensor.transpose(p_cen[:, b * D:(b + 1) * D], t_sq[:, b * P:(b + 1) * P], ident[:])
                    last.then_inc(last_z, 1)

            def chunk(p, c, posted):
                first = isinstance(c, int)
                if p > 0 and first:
                    gen(p, 0)
                    gen(p, 1)
                for t in range(TILES):
                    if p == 0:
                        if first and t % (TILES // X_PARTS) == 0:
                            pe.wait_ge(x_loaded[t * X_PARTS // TILES], 16)
                        tile_whole(c, t)
                    else:
                        if first:
                            pe.wait_ge(gen_lo, (p - 1) * TILES + t + 1)
                        tile_split(p, c, t)
                    if posted:
                        post(*posted, t)
                    if p > 0 and first and t + 2 < TILES:
                        gen(p, t + 2)

            for p in range(PASSES):
                chunk(p, 0, (p - 1, CHUNKS - 1) if p else None)
                if p == 0:
                    pe.wait_ge(center_ready, 1)
                    pe.wait_ge(consts_ready, 3)
                    pe.wait_ge(w_loaded, 16 * len(WEIGHTS))
                    pe.wait_ge(xt_loaded, 16)
                with pe.Fori(1, CHUNKS) as c:
                    chunk(p, c, (p, c - 1))
            for t in range(TILES):
                post(LAST, CHUNKS - 1, t)

        @block.scalar
        def _(act):
            for i in range(X_PARTS):
                part = slice(i * N // X_PARTS, (i + 1) * N // X_PARTS)
                act.dma_start(hidden[:, part], x_blocks[:, part]).then_inc(x_loaded[i], 16)
            for dst, src in WEIGHTS:
                act.dma_start(dst, src).then_inc(w_loaded, 16)
            act.dma_start(xT[:], x_t).then_inc(xt_loaded, 16)

            def gen(p, t):
                n = (p - 1) * TILES + t
                value = p_gen[:, t % 2, 0:GW]
                if p == LAST:
                    half = slice(t % 2 * GW, (t % 2 + 1) * GW)
                    act.wait_ge(zb_ready, t + 1)
                    nc.scalar.activation(t_std[:, half], t_y[:, half], ACT.Silu).then_inc(swish_ready, 1)
                    act.wait_ge(swish_ready, t + 1)
                    value = t_std[:, half]
                else:
                    act.wait_ge(gen_done, n + 1)
                nc.scalar.copy(op_tile(op_hi, t), value).then_inc(gen_hi, 1)

            def hi_tile(p, c, t):
                wait_loaded(act, p, c, t)
                act.wait_ge(tile_used, (p * CHUNKS + c) * TILES + t + 1 - SPLITS)
                nc.scalar.copy(adj_hi[:, t % SPLITS, :], raw_tile(c, t)).then_inc(hi_ready, 1)

            def post(p, c, at):
                chunk_ended = (p * CHUNKS + c + 1) * TILES
                if p in RELU_PASSES and at == 3:
                    act.wait_ge(tile_used, chunk_ended)
                    bias = {1: bias_l1, 3: bias_2}[p]
                    nc.scalar.activation(t_in[:], bank_of(c), ACT.Relu, bias=bias[:]).then_inc(relu_ready, 1)
                if p in NORM_PASSES:
                    n = nth(NORM_PASSES, p, c)
                    if at == (8 if p == 0 else 6):
                        act.wait_ge(cen_done, n + 1)
                        nc.scalar.activation(t_sq[:], p_cen[:], ACT.Square).then_inc(sq_ready, 1)
                    if at == (10 if p == 0 else 8):
                        act.wait_ge(var_done, n + 1)
                        nc.scalar.activation(t_std[:], p_var[:], ACT.Sqrt, bias=eps[:]).then_inc(std_ready, 1)
                if p in HIDDEN_PASSES and at == 3:
                    act.wait_ge(tile_used, chunk_ended)
                    if p == 2:
                        nc.scalar.activation(chunk_of(hidden, c), bank_of(c), ACT.Relu,
                                             bias=bias_1[:]).then_inc(hidden_ready, 1)
                    else:
                        nc.scalar.copy(chunk_of(hidden, c), bank_of(c)).then_inc(hidden_ready, 1)
                if p == LAST:
                    if at == 1:
                        nc.scalar.copy(t_sq[:], chunk_of(xT, c)).then_inc(last_in, 1)
                    if at == 3:
                        act.wait_ge(tile_used, chunk_ended)
                        nc.scalar.copy(t_in[:], bank_of(c)).then_inc(last_in, 1)
                    if at == 6:
                        act.wait_ge(last_zb, c + 1)
                        nc.scalar.activation(t_std[:], t_y[:], ACT.Silu).then_inc(last_act, 1)
                    if at == 13:
                        act.wait_ge(last_out, BPC * (c + 1))
                        act.dma_start(out[bass.ds(c * CW, CW), :].rearrange("(b p) d -> p b d", p=P),
                                      deg_part[:, 0:CW].rearrange("p (b d) -> p b d", b=BPC)).then_inc(stored, 16)
                    if at == 15:
                        act.wait_ge(stored, 16 * (c + 1))

            def chunk(p, c, posted):
                for t in range(TILES):
                    if p > 0 and isinstance(c, int) and t >= 2:
                        gen(p, t - 2)
                    if posted:
                        post(*posted, t)
                    if p > 0:
                        hi_tile(p, c, t)
                if p > 0 and isinstance(c, int):
                    gen(p, TILES - 2)
                    gen(p, TILES - 1)

            act.wait_ge(consts_ready, 3)
            act.wait_ge(w_loaded, 16 * len(WEIGHTS))
            for p in range(PASSES):
                if p > 0:
                    chunk(p, 0, (p - 1, CHUNKS - 1))
                with act.Fori(1, CHUNKS) as c:
                    chunk(p, c, (p, c - 1))
            for t in range(TILES):
                post(LAST, CHUNKS - 1, t)

        @block.vector
        def _(dve):
            dve.wait_ge(ident_ready, 1)
            nc.vector.tensor_scalar(center[:], ident[:], -1.0 / D, None, ALU.add).then_inc(center_ready, 1)

            def gen_bias(t):
                half = slice(t % 2 * GW, (t % 2 + 1) * GW)
                dve.wait_ge(gen_done, (LAST - 1) * TILES + t + 1)
                nc.vector.tensor_tensor(t_y[:, half].rearrange("p (b d) -> p b d", b=BPT),
                                        p_gen[:, t % 2, 0:GW].rearrange("p (b d) -> p b d", b=BPT),
                                        b3_rows[:].unsqueeze(1).broadcast_to([P, BPT, D]),
                                        ALU.add).then_inc(zb_ready, 1)

            def gen(p, t):
                dve.wait_ge(gen_hi, (p - 1) * TILES + t + 1)
                value = t_std[:, t % 2 * GW:(t % 2 + 1) * GW] if p == LAST else p_gen[:, t % 2, 0:GW]
                nc.vector.tensor_tensor(op_tile(op_lo, t), value, op_tile(op_hi, t).bitcast(fp32),
                                        ALU.subtract).then_inc(gen_lo, 1)

            def degree_tile(c, t):
                wait_loaded(dve, 0, c, t)
                if t == 0:
                    if not isinstance(c, int):
                        dve.wait_ge(deg_ready, c)
                    nc.vector.tensor_copy(deg_part[:], raw_tile(c, t)).then_inc(vec_tile, 1)
                else:
                    dve.wait_ge(vec_tile, c * TILES + t)
                    nc.vector.tensor_tensor(deg_part[:], deg_part[:], raw_tile(c, t), ALU.add).then_inc(vec_tile, 1)

            def lo_tile(p, c, t):
                s = t % SPLITS
                dve.wait_ge(hi_ready, ((p - 1) * CHUNKS + c) * TILES + t + 1)
                nc.vector.tensor_tensor(adj_lo[:, s, :], raw_tile(c, t), adj_hi[:, s, :].bitcast(fp32),
                                        ALU.subtract).then_inc(vec_tile, 1)

            def post(p, c, at):
                if p == 0 and at == 3:
                    dve.wait_ge(deg_done, c + 1)
                    nc.vector.tensor_scalar(t_std[:], p_deg[:], float(D), 1.0, ALU.mult, ALU.max).then_inc(deg_step, 1)
                    dve.wait_ge(deg_step, 2 * c + 1)
                    nc.vector.reciprocal(t_std[:], t_std[:]).then_inc(deg_step, 1)
                    dve.wait_ge(deg_step, 2 * c + 2)
                    dve.wait_ge(tile_used, (c + 1) * TILES)
                    nc.vector.tensor_tensor(t_in[:], bank_of(c), t_std[:], ALU.mult).then_inc(neigh_ready, 1)
                if p in NORM_PASSES:
                    n = nth(NORM_PASSES, p, c)
                    if p == 0 and at == 6:
                        dve.wait_ge(mix_done, c + 1)
                        nc.vector.tensor_tensor(t_y[:], p_mix[:], chunk_of(xT, c), ALU.add).then_inc(y_ready, 1)
                    if p != 0 and at == 4:
                        dve.wait_ge(relu_ready, nth(RELU_PASSES, p, c) + 1)
                        nc.vector.tensor_tensor(t_y[:], t_in[:], chunk_of(xT, c), ALU.add).then_inc(y_ready, 1)
                    if at == (11 if p == 0 else 9):
                        dve.wait_ge(std_ready, n + 1)
                        nc.vector.reciprocal(t_std[:], t_std[:]).then_inc(inv_ready, 1)
                        dve.wait_ge(inv_ready, n + 1)
                        nc.vector.tensor_tensor(chunk_of(xT, c), p_cen[:], t_std[:], ALU.mult).then_inc(x_ready, 1)
                if p == LAST and at == 4:
                    dve.wait_ge(last_z, c + 1)
                    nc.vector.tensor_tensor(t_y[:].rearrange("p (b d) -> p b d", b=BPC),
                                            p_mix[:].rearrange("p (b d) -> p b d", b=BPC),
                                            b3_rows[:].unsqueeze(1).broadcast_to([P, BPC, D]),
                                            ALU.add).then_inc(last_zb, 1)
                if p == LAST and at == 8:
                    dve.wait_ge(last_act, c + 1)
                    nc.vector.tensor_tensor(t_y[:], t_std[:], p_cen[:], ALU.add).then_inc(last_y, 1)
                    dve.wait_ge(last_y, c + 1)
                    for b in range(BPC):
                        nc.vector.bn_stats(stats[:, b, :], t_y[:, b * D:(b + 1) * D]).then_inc(last_stats, 1)
                    dve.wait_ge(last_stats, BPC * (c + 1))
                    nc.vector.tensor_copy(mean_even[:], stats[:, :, 1]).then_inc(last_moments, 1)
                    for b in range(BPC):
                        nc.vector.bn_aggr(moments[:, b, :], stats[:, b, :]).then_inc(last_moments, 1)
                    dve.wait_ge(last_moments, (BPC + 1) * (c + 1))
                    nc.vector.tensor_scalar(var_eps[:], moments[:, :, 1], EPS, None, ALU.add).then_inc(last_var, 1)
                if p == LAST and at == 12:
                    dve.wait_ge(last_rstd, c + 1)
                    for b in range(BPC):
                        nc.vector.tensor_scalar(deg_part[:, b * D:(b + 1) * D], t_y[:, b * D:(b + 1) * D],
                                                moments[:, b, 0:1], rstd[:, b:b + 1],
                                                ALU.subtract, ALU.mult).then_inc(last_out, 1)

            def chunk(p, c, posted):
                first = isinstance(c, int)
                for t in range(TILES):
                    if p == LAST and first and t >= 1:
                        gen_bias(t - 1)
                    if p > 0 and first and t >= 2:
                        gen(p, t - 2)
                    if posted:
                        post(*posted, t)
                    if p == 0:
                        degree_tile(c, t)
                    else:
                        lo_tile(p, c, t)
                if p == LAST and first:
                    gen_bias(TILES - 1)
                if p > 0 and first:
                    gen(p, TILES - 2)
                    gen(p, TILES - 1)
                if p == 0:
                    dve.wait_ge(vec_tile, (c + 1) * TILES)
                    nc.vector.tensor_tensor(deg_sum[:], deg_part[:, 0:CW], deg_part[:, CW:2 * CW],
                                            ALU.add).then_inc(deg_ready, 1)

            for p in range(PASSES):
                chunk(p, 0, (p - 1, CHUNKS - 1) if p else None)
                if p == 0:
                    dve.wait_ge(xt_loaded, 16)
                    dve.wait_ge(w_loaded, 16 * len(WEIGHTS))
                with dve.Fori(1, CHUNKS) as c:
                    chunk(p, c, (p, c - 1))
            for t in range(TILES):
                post(LAST, CHUNKS - 1, t)

        @block.gpsimd
        def _(pool):
            nc.gpsimd.memset(ident[:], 0.0).then_inc(ident_zeroed, 1)
            pool.wait_ge(ident_zeroed, 1)
            nc.gpsimd.affine_select(out=ident[:], in_=ident[:], compare_op=ALU.not_equal, fill=1.0, base=0,
                                    pattern=[[-1, P]], channel_multiplier=1).then_inc(ident_ready, 1)
            nc.gpsimd.memset(mean_of[:], 1.0 / D).then_inc(consts_ready, 1)
            nc.gpsimd.memset(minus_half[:], -0.5).then_inc(consts_ready, 1)
            nc.gpsimd.memset(eps[:], EPS).then_inc(consts_ready, 1)
            pool.wait_ge(consts_ready, 3)
            with pool.Fori(0, CHUNKS) as c:
                pool.wait_ge(last_var, c + 1)
                nc.gpsimd.tensor_tensor(rstd[:], var_eps[:], minus_half[:], ALU.pow).then_inc(last_rstd, 1)


def kernel(x, adj, L0_gnn_W_self, L0_gnn_W_neigh, L1_gnn_kernel, L1_gnn_bias, L2_gnn_W1, L2_gnn_b1, L2_gnn_W2,
           L2_gnn_b2, L3_gnn_W, L3_gnn_b):
    import numpy as _np
    import concourse.bacc as _bacc
    from concourse import mybir as _mybir
    from concourse.bass_utils import run_bass_kernel_spmd as _run

    P, CW, BPT = 128, 512, 2
    x, adj = _np.asarray(x), _np.asarray(adj)
    n, d = x.shape
    tiles = adj.T.reshape(n // (BPT * P), BPT, P, n // CW, CW).transpose(3, 0, 2, 1, 4)
    arrays = {
        "adj_tiles": tiles.reshape(n // CW, n // (BPT * P), P, BPT * CW),
        "x_blocks": x.reshape(n // P, P, d).transpose(1, 0, 2).reshape(P, n * d // P),
        "x_t": x.T,
        "W_self": L0_gnn_W_self, "W_neigh": L0_gnn_W_neigh, "L1_kernel": L1_gnn_kernel,
        "L1_bias": _np.asarray(L1_gnn_bias).reshape(d, 1), "W1": L2_gnn_W1,
        "b1": _np.asarray(L2_gnn_b1).reshape(d, 1), "W2": L2_gnn_W2, "b2": _np.asarray(L2_gnn_b2).reshape(d, 1),
        "L3_W": L3_gnn_W, "L3_b": _np.asarray(L3_gnn_b),
    }
    arrays = {name: _np.ascontiguousarray(a) for name, a in arrays.items()}
    nc = _bacc.Bacc("TRN2", target_bir_lowering=False, num_devices=1)
    args = [nc.dram_tensor(name, a.shape, _mybir.dt.from_np(a.dtype), kind="ExternalInput").ap()
            for name, a in arrays.items()]
    args.append(nc.dram_tensor("out", (n, d), _mybir.dt.float32, kind="ExternalOutput").ap())
    bass_gnn_residual_norm_kernel(nc, *args)
    r = _run(nc, [arrays], core_ids=[0])
    return r.results[0]["out"]
```

```python
import concourse.bass as bass
from concourse import mybir
from contextlib import ExitStack


def bass_gnn_residual_norm_kernel(
    nc: bass.Bass,
    adj_tiles: bass.AP,
    x_blocks: bass.AP,
    x_t: bass.AP,
    W_self: bass.AP,
    W_neigh: bass.AP,
    L1_kernel: bass.AP,
    L1_bias: bass.AP,
    W1: bass.AP,
    b1: bass.AP,
    W2: bass.AP,
    b2: bass.AP,
    L3_W: bass.AP,
    L3_b: bass.AP,
    out: bass.AP,
):
    fp32 = mybir.dt.float32
    fp32r = mybir.dt.float32r
    ALU = mybir.AluOpType
    ACT = mybir.ActivationFunctionType
    P = 128

    D = x_t.shape[0]
    N = x_t.shape[1]
    CHUNKS, TILES = adj_tiles.shape[0], adj_tiles.shape[1]
    NB = N // P
    CW = N // CHUNKS
    BPT = NB // TILES
    TW = BPT * CW
    BPC = CW // P
    GW = BPT * D
    PASSES = 6
    SLOTS = 7
    STREAMED = 2 * SLOTS
    KEPT = TILES - STREAMED
    LOADS = STREAMED // SLOTS
    SPLITS = 4
    X_PARTS = 4
    EPS = 1e-5
    NORM_PASSES = [0, 1, 3]
    STATS_PASSES = NORM_PASSES + [5]
    RELU_PASSES = [1, 3]
    HIDDEN_PASSES = [2, 4]
    LAST = PASSES - 1

    ctx = ExitStack()
    with ctx:
        def sb(name, shape, dt=fp32):
            return ctx.enter_context(nc.sbuf_tensor(name, shape, dt))

        def pb(name, shape):
            return ctx.enter_context(nc.psum_tensor(name, shape, fp32))

        def sem(name):
            return ctx.enter_context(nc.semaphore(name))

        xT = sb("xT", [P, N])
        hidden = sb("hidden", [P, N])
        op_hi = sb("op_hi", [P, N], fp32r)
        op_lo = sb("op_lo", [P, N], fp32r)
        kept = sb("kept", [P, CHUNKS * KEPT, TW])   
        ring = sb("ring", [P, SLOTS, TW])
        adj_hi = sb("adj_hi", [P, SPLITS, TW], fp32r)
        adj_lo = sb("adj_lo", [P, SPLITS, TW], fp32r)
        w_self = sb("w_self", [P, D])
        w_neigh = sb("w_neigh", [P, D])
        w_l1 = sb("w_l1", [P, D])
        w_1 = sb("w_1", [P, D])
        w_2 = sb("w_2", [P, D])
        w_3 = sb("w_3", [P, D])
        b3_rows = sb("b3_rows", [P, D])
        bias_l1 = sb("bias_l1", [P, 1])
        bias_1 = sb("bias_1", [P, 1])
        bias_2 = sb("bias_2", [P, 1])
        ident = sb("ident", [P, P])
        ones = sb("ones", [P, 1])
        deg_part = sb("deg_part", [P, TW])
        deg_sum = sb("deg_sum", [P, CW])
        t_in = sb("t_in", [P, CW])
        t_x = sb("t_x", [P, CW])
        t_y = sb("t_y", [P, CW])
        t_act = sb("t_act", [P, CW])
        rdeg = sb("rdeg", [P, BPC])
        stats = sb("stats", [P, BPC, 6])
        moments = sb("moments", [P, BPC, 2])
        var_eps = sb("var_eps", [P, BPC])
        rstd = sb("rstd", [P, BPC])
        shift = sb("shift", [P, BPC])
        minus_half = sb("minus_half", [P, BPC])

        WEIGHTS = [(w_self[:], W_self), (w_neigh[:], W_neigh), (w_l1[:], L1_kernel), (w_1[:], W1), (w_2[:], W2),
                   (w_3[:], L3_W), (bias_l1[:], L1_bias), (bias_1[:], b1), (bias_2[:], b2),
                   (b3_rows[:], L3_b.partition_broadcast(P))]

        agg = pb("agg", [P, 2 * CW])
        p_gen = pb("p_gen", [P, 2, 512])
        p_deg = pb("p_deg", [P, BPC])
        p_mix = pb("p_mix", [P, CW])
        p_rows = pb("p_rows", [P, CW])
        p_turn = pb("p_turn", [P, CW])

        x_loaded = [sem(f"x_loaded{i}") for i in range(X_PARTS)]
        x_moved = sem("x_moved")
        w_loaded = sem("w_loaded")
        slot_loaded = [sem(f"slot_loaded{s}") for s in range(SLOTS)]
        kept_loaded = sem("kept_loaded")
        ident_zeroed = sem("ident_zeroed")
        ident_ready = sem("ident_ready")
        consts_ready = sem("consts_ready")
        tile_used = sem("tile_used")
        vec_tile = sem("vec_tile")
        hi_ready = sem("hi_ready")
        deg_ready = sem("deg_ready")
        deg_step = sem("deg_step")
        copies_ready = sem("copies_ready")
        mix_done = sem("mix_done")
        scaled_ready = sem("scaled_ready")
        y_half = sem("y_half")
        relu_ready = sem("relu_ready")
        y_ready = sem("y_ready")
        rows_done = sem("rows_done")
        stats_ready = sem("stats_ready")
        moments_ready = sem("moments_ready")
        var_ready = sem("var_ready")
        rstd_ready = sem("rstd_ready")
        shift_ready = sem("shift_ready")
        norm_ready = sem("norm_ready")
        turn_done = sem("turn_done")
        x_ready = sem("x_ready")
        hidden_ready = sem("hidden_ready")
        gen_done = sem("gen_done")
        zb_ready = sem("zb_ready")
        swish_ready = sem("swish_ready")
        gen_hi = sem("gen_hi")
        gen_lo = sem("gen_lo")
        last_in = sem("last_in")
        last_z = sem("last_z")
        last_zb = sem("last_zb")
        last_act = sem("last_act")
        last_y = sem("last_y")
        last_out = sem("last_out")

        ENTRY_AT = 3
        RESIDUAL_AT = {0: 8, 1: 4, 3: 4}
        ROWS_AT = {0: 1, 1: 2, 3: 2, 5: 2}
        STATS_AT = {0: 9, 1: 7, 3: 7, 5: 10}
        MOMENTS_AT = {0: 10, 1: 8, 3: 8, 5: 11}
        SHIFT_AT = {0: 12, 1: 10, 3: 10}
        NORM_AT = {0: 12, 1: 11, 3: 11}
        TURN_AT = {0: 11, 1: 9, 3: 9}
        X_AT = {0: 14, 1: 13, 3: 13}
        LATE = CW // P // BPT
        EARLY = TILES - LATE
        GEN_LAG = 5

        block = ctx.enter_context(nc.Block())

        def nth(passes, p, c):
            return passes.index(p) * CHUNKS + c

        def chunk_of(t, c):
            return t[:, bass.ds(c * CW, CW)]

        def bank_of(c):
            return agg[:, bass.ds((c % 2) * CW, CW)]

        def raw_tile(c, t):
            if t < STREAMED:
                return ring[:, t % SLOTS, :]
            return kept[:, bass.ds(c * KEPT + t - STREAMED, 1), :].rearrange("p o n -> p (o n)")

        def op_tile(buf, t):
            return buf[:, t * GW:(t + 1) * GW]

        def wait_loaded(eng, p, c, t):
            if t < STREAMED:
                eng.wait_ge(slot_loaded[t % SLOTS], 16 * (LOADS * (p * CHUNKS + c) + t // SLOTS + 1))
            elif t == STREAMED and p == 0:
                eng.wait_ge(kept_loaded, 16 * (c + 1))

        @block.sync
        def _(sp):
            def load_chunk(p, c):
                first = isinstance(c, int) and c == 0
                for t in range(STREAMED):
                    before = (p * CHUNKS + c) * TILES + t + 1 - SLOTS - (KEPT if t < SLOTS else 0)
                    if not (p == 0 and first and t < SLOTS):
                        if p == 0 or (p == 1 and first and t < SLOTS):
                            sp.wait_ge(tile_used, before)
                        sp.wait_ge(vec_tile, before)
                    sp.dma_start(ring[:, t % SLOTS, :], adj_tiles[c, t]).then_inc(slot_loaded[t % SLOTS], 16)
                if p == 0:
                    if not first:
                        sp.wait_ge(kept_loaded, 16 * c)
                    sp.dma_start(kept[:, bass.ds(c * KEPT, KEPT), :],
                                 adj_tiles[c, STREAMED:TILES].rearrange("t p n -> p t n")).then_inc(kept_loaded, 16)

            for p in range(PASSES):
                load_chunk(p, 0)
                with sp.Fori(1, CHUNKS) as c:
                    load_chunk(p, c)

        @block.tensor
        def _(pe):
            def gen(p, t):
                c_of = t * BPT // BPC
                if p in (1, 2, 4):
                    src = xT
                    pe.wait_ge(x_ready, nth(NORM_PASSES, {1: 0, 2: 1, 4: 3}[p], c_of) + 1)
                else:
                    src = hidden
                    pe.wait_ge(hidden_ready, nth(HIDDEN_PASSES, p - 1, c_of) + 1)
                if (p - 1) * TILES + t >= 2:
                    pe.wait_ge(gen_lo, (p - 1) * TILES + t - 1)
                for b in range(BPT):
                    j = t * BPT + b
                    dst = p_gen[:, t % 2, b * D:(b + 1) * D]
                    if p == 4:
                        last = nc.tensor.transpose(dst, src[:, j * P:(j + 1) * P], ident[:])
                    else:
                        w = {1: w_l1, 2: w_1, 3: w_2, 5: w_3}[p]
                        last = nc.tensor.matmul(dst, src[:, j * P:(j + 1) * P], w[:], start=True, stop=True)
                last.then_inc(gen_done, 1)

            def tile_whole(c, t):
                wait_loaded(pe, 0, c, t)
                raw = raw_tile(c, t)
                for b in range(BPT):
                    j = t * BPT + b
                    last = nc.tensor.matmul(bank_of(c), hidden[:, j * D:(j + 1) * D],
                                            raw[:, b * CW:(b + 1) * CW], start=(j == 0), stop=(j == NB - 1))
                last.then_inc(tile_used, 1)

            def tile_split(p, c, t):
                s = t % SPLITS
                pe.wait_ge(hi_ready, ((p - 1) * CHUNKS + c) * TILES + t + 1)
                for b in range(BPT):
                    j = t * BPT + b
                    a_hi = adj_hi[:, s, b * CW:(b + 1) * CW]
                    nc.tensor.matmul(bank_of(c), op_hi[:, j * D:(j + 1) * D], a_hi, start=(j == 0), stop=False)
                    nc.tensor.matmul(bank_of(c), op_lo[:, j * D:(j + 1) * D], a_hi, start=False, stop=False)
                pe.wait_ge(vec_tile, (p * CHUNKS + c) * TILES + t + 1)
                for b in range(BPT):
                    j = t * BPT + b
                    last = nc.tensor.matmul(bank_of(c), op_hi[:, j * D:(j + 1) * D],
                                            adj_lo[:, s, b * CW:(b + 1) * CW], start=False, stop=(j == NB - 1))
                last.then_inc(tile_used, 1)

            def post(p, c, at):
                if p == 0 and at == ROWS_AT[p]:
                    pe.wait_ge(deg_ready, c + 1)
                    pe.wait_ge(copies_ready, 2 * (c + 1))
                    for b in range(BPC):
                        blk = slice(b * P, (b + 1) * P)
                        nc.tensor.matmul(p_deg[:, b:b + 1], deg_sum[:, blk], ones[:], start=True, stop=True)
                        nc.tensor.matmul(p_mix[:, blk], t_in[:, blk], w_neigh[:], start=True, stop=True)
                        nc.tensor.matmul(p_rows[:, blk], t_x[:, blk], w_self[:], start=True, stop=True)
                        last = nc.tensor.transpose(p_turn[:, blk], t_x[:, blk], ident[:])
                    last.then_inc(mix_done, 1)
                if p in RELU_PASSES and at == ROWS_AT[p]:
                    pe.wait_ge(y_ready, nth(NORM_PASSES, p, c) + 1)
                    for b in range(BPC):
                        last = nc.tensor.transpose(p_rows[:, b * D:(b + 1) * D], t_y[:, b * P:(b + 1) * P], ident[:])
                    last.then_inc(rows_done, 1)
                if p in NORM_PASSES and at == TURN_AT[p]:
                    pe.wait_ge(norm_ready, BPC * (nth(NORM_PASSES, p, c) + 1))
                    for b in range(BPC):
                        last = nc.tensor.transpose(p_turn[:, b * P:(b + 1) * P], t_x[:, b * D:(b + 1) * D], ident[:])
                    last.then_inc(turn_done, 1)
                if p in HIDDEN_PASSES and at == 6:
                    pe.wait_ge(hidden_ready, nth(HIDDEN_PASSES, p, c) + 1)
                if p == LAST and at == ROWS_AT[p]:
                    pe.wait_ge(last_in, 2 * (c + 1))
                    for b in range(BPC):
                        nc.tensor.matmul(p_mix[:, b * D:(b + 1) * D], t_in[:, b * P:(b + 1) * P], w_3[:],
                                         start=True, stop=True)
                    for b in range(BPC):
                        last = nc.tensor.transpose(p_turn[:, b * D:(b + 1) * D], t_x[:, b * P:(b + 1) * P], ident[:])
                    last.then_inc(last_z, 1)

            def chunk(p, c, posted):
                first = isinstance(c, int) and c == 0
                final = isinstance(c, int) and c == CHUNKS - 1
                for t in range(TILES):
                    if p == 0:
                        if first and t % (TILES // X_PARTS) == 0:
                            pe.wait_ge(x_loaded[t * X_PARTS // TILES], 16)
                        tile_whole(c, t)
                    else:
                        if first and (t == 0 or t >= EARLY):
                            ready = EARLY if t < EARLY else t + 1
                            pe.wait_ge(gen_lo, (p - 1) * TILES + ready)
                        tile_split(p, c, t)
                    if posted:
                        post(*posted, t)
                    if p > 0 and first and t + 2 >= EARLY and t + 2 < TILES:
                        gen(p, t + 2)
                    if p < LAST and final and t < EARLY:
                        gen(p + 1, t)

            for p in range(PASSES):
                chunk(p, 0, (p - 1, CHUNKS - 1) if p else None)
                if p == 0:
                    pe.wait_ge(ident_ready, 1)
                    pe.wait_ge(consts_ready, 2)
                    pe.wait_ge(w_loaded, 16 * len(WEIGHTS))
                with pe.Fori(1, CHUNKS - 1) as c:
                    chunk(p, c, (p, c - 1))
                chunk(p, CHUNKS - 1, (p, CHUNKS - 2))
            for t in range(TILES):
                post(LAST, CHUNKS - 1, t)

        @block.scalar
        def _(act):
            for i in range(X_PARTS):
                part = slice(i * N // X_PARTS, (i + 1) * N // X_PARTS)
                act.dma_start(hidden[:, part], x_blocks[:, part]).then_inc(x_loaded[i], 16)
            for dst, src in WEIGHTS:
                act.dma_start(dst, src).then_inc(w_loaded, 16)
            act.wait_ge(tile_used, TILES // 2)
            act.dma_start(xT[:], x_t).then_inc(x_moved, 16)

            def gen(p, t):
                n = (p - 1) * TILES + t
                value = p_gen[:, t % 2, 0:GW]
                if p == LAST:
                    half = slice(t % 2 * GW, (t % 2 + 1) * GW)
                    act.wait_ge(zb_ready, t + 1)
                    nc.scalar.activation(t_act[:, half], t_y[:, half], ACT.Silu).then_inc(swish_ready, 1)
                    act.wait_ge(swish_ready, t + 1)
                    value = t_act[:, half]
                else:
                    act.wait_ge(gen_done, n + 1)
                nc.scalar.copy(op_tile(op_hi, t), value).then_inc(gen_hi, 1)

            def hi_tile(p, c, t):
                wait_loaded(act, p, c, t)
                act.wait_ge(tile_used, (p * CHUNKS + c) * TILES + t + 1 - SPLITS)
                nc.scalar.copy(adj_hi[:, t % SPLITS, :], raw_tile(c, t)).then_inc(hi_ready, 1)

            def post(p, c, at):
                chunk_ended = (p * CHUNKS + c + 1) * TILES
                if p == 0 and at == ENTRY_AT:
                    nc.scalar.copy(t_x[:], chunk_of(xT, c)).then_inc(copies_ready, 1)
                    act.wait_ge(tile_used, chunk_ended)
                    nc.scalar.copy(t_in[:], bank_of(c)).then_inc(copies_ready, 1)
                if p == 0 and at == 7:
                    act.wait_ge(deg_step, 2 * (c + 1))
                    for b in range(BPC):
                        nc.scalar.activation(t_act[:, b * D:(b + 1) * D], p_mix[:, b * D:(b + 1) * D], ACT.Copy,
                                             scale=rdeg[:, b:b + 1]).then_inc(scaled_ready, 1)
                if p in RELU_PASSES and at == ENTRY_AT:
                    act.wait_ge(tile_used, chunk_ended)
                    bias = {1: bias_l1, 3: bias_2}[p]
                    nc.scalar.activation(t_in[:], bank_of(c), ACT.Relu, bias=bias[:]).then_inc(relu_ready, 1)
                if p in NORM_PASSES and at == NORM_AT[p]:
                    act.wait_ge(shift_ready, nth(NORM_PASSES, p, c) + 1)
                    rows = t_y if p == 0 else p_rows
                    for b in range(BPC):
                        nc.scalar.activation(t_x[:, b * D:(b + 1) * D], rows[:, b * D:(b + 1) * D], ACT.Identity,
                                             bias=shift[:, b:b + 1], scale=rstd[:, b:b + 1]).then_inc(norm_ready, 1)
                if p in NORM_PASSES and at == X_AT[p]:
                    act.wait_ge(turn_done, nth(NORM_PASSES, p, c) + 1)
                    act.nop(nofuse=True)
                    nc.scalar.copy(chunk_of(xT, c), p_turn[:]).then_inc(x_ready, 1)
                if p in HIDDEN_PASSES and at == ENTRY_AT:
                    act.wait_ge(tile_used, chunk_ended)
                    if p == 2:
                        nc.scalar.activation(chunk_of(hidden, c), bank_of(c), ACT.Relu,
                                             bias=bias_1[:]).then_inc(hidden_ready, 1)
                    else:
                        nc.scalar.copy(chunk_of(hidden, c), bank_of(c)).then_inc(hidden_ready, 1)
                if p == LAST:
                    if at == ENTRY_AT - 1:
                        nc.scalar.copy(t_x[:], chunk_of(xT, c)).then_inc(last_in, 1)
                    if at == ENTRY_AT:
                        act.wait_ge(tile_used, chunk_ended)
                        nc.scalar.copy(t_in[:], bank_of(c)).then_inc(last_in, 1)
                    if at == 8:
                        act.wait_ge(last_zb, c + 1)
                        nc.scalar.activation(t_act[:], t_y[:], ACT.Silu).then_inc(last_act, 1)
                    if at == 15:
                        act.wait_ge(last_out, BPC * (c + 1))
                        act.dma_start(out[bass.ds(c * CW, CW), :].rearrange("(b p) d -> p b d", p=P),
                                      deg_part[:, 0:CW].rearrange("p (b d) -> p b d", b=BPC)).then_inc(x_moved, 16)

            def chunk(p, c, posted):
                first = isinstance(c, int) and c == 0
                final = isinstance(c, int) and c == CHUNKS - 1
                for t in range(TILES + GEN_LAG):
                    if p < LAST and final and 0 <= t - GEN_LAG < EARLY:
                        gen(p + 1, t - GEN_LAG)
                    if p > 0 and first and EARLY <= t - 1 < TILES:
                        gen(p, t - 1)
                    if posted and t < TILES:
                        post(*posted, t)
                    if p > 0 and t < TILES:
                        hi_tile(p, c, t)

            act.wait_ge(x_moved, 16)
            act.wait_ge(w_loaded, 16 * len(WEIGHTS))
            for p in range(PASSES):
                if p > 0:
                    chunk(p, 0, (p - 1, CHUNKS - 1))
                with act.Fori(1, CHUNKS - 1) as c:
                    chunk(p, c, (p, c - 1))
                chunk(p, CHUNKS - 1, (p, CHUNKS - 2))
            for t in range(TILES):
                post(LAST, CHUNKS - 1, t)
            act.wait_ge(x_moved, 16 * (CHUNKS + 1))

        @block.vector
        def _(dve):
            def gen_bias(t):
                half = slice(t % 2 * GW, (t % 2 + 1) * GW)
                dve.wait_ge(gen_done, (LAST - 1) * TILES + t + 1)
                nc.vector.tensor_tensor(t_y[:, half].rearrange("p (b d) -> p b d", b=BPT),
                                        p_gen[:, t % 2, 0:GW].rearrange("p (b d) -> p b d", b=BPT),
                                        b3_rows[:].unsqueeze(1).broadcast_to([P, BPT, D]),
                                        ALU.add).then_inc(zb_ready, 1)

            def gen(p, t):
                dve.wait_ge(gen_hi, (p - 1) * TILES + t + 1)
                value = t_act[:, t % 2 * GW:(t % 2 + 1) * GW] if p == LAST else p_gen[:, t % 2, 0:GW]
                nc.vector.tensor_tensor(op_tile(op_lo, t), value, op_tile(op_hi, t).bitcast(fp32),
                                        ALU.subtract).then_inc(gen_lo, 1)

            def degree_tile(c, t):
                wait_loaded(dve, 0, c, t)
                if t == 0:
                    if not (isinstance(c, int) and c == 0):
                        dve.wait_ge(deg_ready, c)
                    nc.vector.tensor_copy(deg_part[:], raw_tile(c, t)).then_inc(vec_tile, 1)
                else:
                    dve.wait_ge(vec_tile, c * TILES + t)
                    nc.vector.tensor_tensor(deg_part[:], deg_part[:], raw_tile(c, t), ALU.add).then_inc(vec_tile, 1)

            def lo_tile(p, c, t):
                s = t % SPLITS
                dve.wait_ge(hi_ready, ((p - 1) * CHUNKS + c) * TILES + t + 1)
                nc.vector.tensor_tensor(adj_lo[:, s, :], raw_tile(c, t), adj_hi[:, s, :].bitcast(fp32),
                                        ALU.subtract).then_inc(vec_tile, 1)

            def post(p, c, at):
                if p == 0 and at == 6:
                    dve.wait_ge(mix_done, c + 1)
                    nc.vector.tensor_scalar(rdeg[:], p_deg[:], 1.0, None, ALU.max).then_inc(deg_step, 1)
                    dve.wait_ge(deg_step, 2 * c + 1)
                    nc.vector.reciprocal(rdeg[:], rdeg[:]).then_inc(deg_step, 1)
                if p == 0 and at == RESIDUAL_AT[p]:
                    dve.wait_ge(scaled_ready, BPC * (c + 1))
                    nc.vector.tensor_tensor(t_y[:], t_act[:], p_rows[:], ALU.add).then_inc(y_half, 1)
                    dve.wait_ge(y_half, c + 1)
                    nc.vector.tensor_tensor(t_y[:], t_y[:], p_turn[:], ALU.add).then_inc(y_ready, 1)
                if p in RELU_PASSES and at == RESIDUAL_AT[p]:
                    dve.wait_ge(relu_ready, nth(RELU_PASSES, p, c) + 1)
                    nc.vector.tensor_tensor(t_y[:], t_in[:], chunk_of(xT, c), ALU.add).then_inc(y_ready, 1)
                if p in STATS_PASSES and at == STATS_AT[p]:
                    n = nth(STATS_PASSES, p, c)
                    rows = p_rows if p in RELU_PASSES else t_y
                    if p == 0:
                        dve.wait_ge(y_ready, nth(NORM_PASSES, p, c) + 1)
                    elif p in RELU_PASSES:
                        dve.wait_ge(rows_done, nth(RELU_PASSES, p, c) + 1)
                    else:
                        dve.wait_ge(last_y, c + 1)
                    for b in range(BPC):
                        nc.vector.bn_stats(stats[:, b, :], rows[:, b * D:(b + 1) * D]).then_inc(stats_ready, 1)
                if p in STATS_PASSES and at == MOMENTS_AT[p]:
                    dve.wait_ge(stats_ready, BPC * (nth(STATS_PASSES, p, c) + 1))
                    dve.nop(nofuse=True)
                    for b in range(BPC):
                        nc.vector.bn_aggr(moments[:, b, :], stats[:, b, :]).then_inc(moments_ready, 1)
                if p in NORM_PASSES and at == SHIFT_AT[p]:
                    dve.wait_ge(rstd_ready, nth(STATS_PASSES, p, c) + 1)
                    nc.vector.scalar_tensor_tensor(out=shift[:], in0=moments[:, :, 0], scalar=-1.0, in1=rstd[:],
                                                   op0=ALU.mult, op1=ALU.mult).then_inc(shift_ready, 1)
                if p == LAST and at == 7:
                    dve.wait_ge(last_z, c + 1)
                    nc.vector.tensor_tensor(t_y[:].rearrange("p (b d) -> p b d", b=BPC),
                                            p_mix[:].rearrange("p (b d) -> p b d", b=BPC),
                                            b3_rows[:].unsqueeze(1).broadcast_to([P, BPC, D]),
                                            ALU.add).then_inc(last_zb, 1)
                if p == LAST and at == 9:
                    dve.wait_ge(last_act, c + 1)
                    nc.vector.tensor_tensor(t_y[:], t_act[:], p_turn[:], ALU.add).then_inc(last_y, 1)
                if p == LAST and at == 13:
                    dve.wait_ge(x_moved, 16 * (c + 1))
                    dve.wait_ge(rstd_ready, nth(STATS_PASSES, p, c) + 1)
                    for b in range(BPC):
                        nc.vector.tensor_scalar(deg_part[:, b * D:(b + 1) * D], t_y[:, b * D:(b + 1) * D],
                                                moments[:, b, 0:1], rstd[:, b:b + 1],
                                                ALU.subtract, ALU.mult).then_inc(last_out, 1)

            def chunk(p, c, posted):
                first = isinstance(c, int) and c == 0
                final = isinstance(c, int) and c == CHUNKS - 1
                for t in range(TILES + GEN_LAG):
                    if p == LAST - 1 and final and 0 <= t - GEN_LAG + 1 < EARLY:
                        gen_bias(t - GEN_LAG + 1)
                    if p < LAST and final and 0 <= t - GEN_LAG < EARLY:
                        gen(p + 1, t - GEN_LAG)
                    if p == LAST and first and EARLY <= t < TILES:
                        gen_bias(t)
                    if p > 0 and first and EARLY <= t - 1 < TILES:
                        gen(p, t - 1)
                    if posted and t < TILES:
                        post(*posted, t)
                    if p == 0 and t < TILES:
                        degree_tile(c, t)
                    elif t < TILES:
                        lo_tile(p, c, t)
                    if p == 0 and t == TILES - 1:
                        dve.wait_ge(vec_tile, (c + 1) * TILES)
                        nc.vector.tensor_tensor(deg_sum[:], deg_part[:, 0:CW], deg_part[:, CW:2 * CW],
                                                ALU.add).then_inc(deg_ready, 1)

            for p in range(PASSES):
                chunk(p, 0, (p - 1, CHUNKS - 1) if p else None)
                if p == 0:
                    dve.wait_ge(w_loaded, 16 * len(WEIGHTS))
                with dve.Fori(1, CHUNKS - 1) as c:
                    chunk(p, c, (p, c - 1))
                chunk(p, CHUNKS - 1, (p, CHUNKS - 2))
            for t in range(TILES):
                post(LAST, CHUNKS - 1, t)

        @block.gpsimd
        def _(pool):
            nc.gpsimd.memset(ident[:], 0.0).then_inc(ident_zeroed, 1)
            pool.wait_ge(ident_zeroed, 1)
            nc.gpsimd.affine_select(out=ident[:], in_=ident[:], compare_op=ALU.not_equal, fill=1.0, base=0,
                                    pattern=[[-1, P]], channel_multiplier=1).then_inc(ident_ready, 1)
            nc.gpsimd.memset(ones[:], 1.0).then_inc(consts_ready, 1)
            nc.gpsimd.memset(minus_half[:], -0.5).then_inc(consts_ready, 1)
            pool.wait_ge(consts_ready, 2)
            with pool.Fori(0, len(STATS_PASSES) * CHUNKS) as n:
                pool.wait_ge(moments_ready, BPC * (n + 1))
                pool.nop(nofuse=True)
                nc.gpsimd.tensor_scalar(var_eps[:], moments[:, :, 1], EPS, None, ALU.add).then_inc(var_ready, 1)
                pool.wait_ge(var_ready, n + 1)
                nc.gpsimd.tensor_tensor(rstd[:], var_eps[:], minus_half[:], ALU.pow).then_inc(rstd_ready, 1)


def kernel(x, adj, L0_gnn_W_self, L0_gnn_W_neigh, L1_gnn_kernel, L1_gnn_bias, L2_gnn_W1, L2_gnn_b1, L2_gnn_W2,
           L2_gnn_b2, L3_gnn_W, L3_gnn_b):
    import numpy as _np
    import concourse.bacc as _bacc
    from concourse import mybir as _mybir
    from concourse.bass_utils import run_bass_kernel_spmd as _run

    P, CW, BPT = 128, 512, 2
    x, adj = _np.asarray(x), _np.asarray(adj)
    n, d = x.shape
    tiles = adj.T.reshape(n // (BPT * P), BPT, P, n // CW, CW).transpose(3, 0, 2, 1, 4)
    arrays = {
        "adj_tiles": tiles.reshape(n // CW, n // (BPT * P), P, BPT * CW),
        "x_blocks": x.reshape(n // P, P, d).transpose(1, 0, 2).reshape(P, n * d // P),
        "x_t": x.T,
        "W_self": L0_gnn_W_self, "W_neigh": L0_gnn_W_neigh, "L1_kernel": L1_gnn_kernel,
        "L1_bias": _np.asarray(L1_gnn_bias).reshape(d, 1), "W1": L2_gnn_W1,
        "b1": _np.asarray(L2_gnn_b1).reshape(d, 1), "W2": L2_gnn_W2, "b2": _np.asarray(L2_gnn_b2).reshape(d, 1),
        "L3_W": L3_gnn_W, "L3_b": _np.asarray(L3_gnn_b),
    }
    arrays = {name: _np.ascontiguousarray(a) for name, a in arrays.items()}
    nc = _bacc.Bacc("TRN2", target_bir_lowering=False, num_devices=1)
    args = [nc.dram_tensor(name, a.shape, _mybir.dt.from_np(a.dtype), kind="ExternalInput").ap()
            for name, a in arrays.items()]
    args.append(nc.dram_tensor("out", (n, d), _mybir.dt.float32, kind="ExternalOutput").ap())
    bass_gnn_residual_norm_kernel(nc, *args)
    r = _run(nc, [arrays], core_ids=[0])
    return r.results[0]["out"]
```

```python
import concourse.bass as bass
from concourse import mybir
from contextlib import ExitStack


def bass_gnn_residual_norm_kernel(
    nc: bass.Bass,
    adj_tiles: bass.AP,
    x_blocks: bass.AP,
    x_t: bass.AP,
    W_self: bass.AP,
    W_neigh: bass.AP,
    L1_kernel: bass.AP,
    L1_bias: bass.AP,
    W1: bass.AP,
    b1: bass.AP,
    W2: bass.AP,
    b2: bass.AP,
    L3_W: bass.AP,
    L3_b: bass.AP,
    out: bass.AP,
):
    fp32 = mybir.dt.float32
    fp32r = mybir.dt.float32r
    ALU = mybir.AluOpType
    ACT = mybir.ActivationFunctionType
    P = 128

    D = x_t.shape[0]
    N = x_t.shape[1]
    CHUNKS, TILES = adj_tiles.shape[0], adj_tiles.shape[1]
    NB = N // P
    CW = N // CHUNKS
    BPT = NB // TILES
    TW = BPT * CW
    BPC = CW // P
    GW = BPT * D
    PASSES = 6
    SLOTS = 7
    STREAMED = 2 * SLOTS
    KEPT = TILES - STREAMED
    LOADS = STREAMED // SLOTS
    SPLITS = 4
    SPLIT_FIRST = [3, 7, 11, 15]
    GEN_BANKS = 3
    X_PARTS = 8
    EPS = 1e-5
    NORM_PASSES = [0, 1, 3, 5]
    TURN_PASSES = [0, 1]
    RELU_PASSES = [1, 3]
    GEN_PASSES = [1, 2, 3, 5]
    HIDDEN_PASSES = [2, 4]
    LAST = PASSES - 1

    ctx = ExitStack()
    with ctx:
        def sb(name, shape, dt=fp32):
            return ctx.enter_context(nc.sbuf_tensor(name, shape, dt))

        def pb(name, shape):
            return ctx.enter_context(nc.psum_tensor(name, shape, fp32))

        def sem(name):
            return ctx.enter_context(nc.semaphore(name))

        xT = sb("xT", [P, N])
        hidden = sb("hidden", [P, N])
        op_hi = sb("op_hi", [P, N], fp32r)
        op_lo = sb("op_lo", [P, N], fp32r)
        kept = sb("kept", [P, CHUNKS * KEPT, TW])
        ring = sb("ring", [P, SLOTS, TW])
        adj_hi = sb("adj_hi", [P, SPLITS, TW], fp32r)
        adj_lo = sb("adj_lo", [P, SPLITS, TW], fp32r)
        w_self = sb("w_self", [P, D])
        w_neigh = sb("w_neigh", [P, D])
        w_l1 = sb("w_l1", [P, D])
        w_1 = sb("w_1", [P, D])
        w_2 = sb("w_2", [P, D])
        w_3 = sb("w_3", [P, D])
        b3_rows = sb("b3_rows", [P, D])
        bias_l1 = sb("bias_l1", [P, 1])
        bias_1 = sb("bias_1", [P, 1])
        bias_2 = sb("bias_2", [P, 1])
        ident = sb("ident", [P, P])
        ones = sb("ones", [P, 1])
        deg_part = sb("deg_part", [P, TW])
        deg_sum = sb("deg_sum", [P, CW])
        t_in = sb("t_in", [P, CW])
        t_x = sb("t_x", [P, CW])
        t_y = sb("t_y", [P, CW])
        t_act = sb("t_act", [P, CW])
        rdeg = sb("rdeg", [P, BPC])
        stats = sb("stats", [P, BPC, 6])
        moments = sb("moments", [P, BPC, 2])
        var_eps = sb("var_eps", [P, BPC])
        rstd = sb("rstd", [P, BPC])
        shift = sb("shift", [P, BPC])
        minus_half = sb("minus_half", [P, BPC])

        WEIGHTS = [(w_self[:], W_self), (w_neigh[:], W_neigh), (w_l1[:], L1_kernel), (w_1[:], W1), (w_2[:], W2),
                   (w_3[:], L3_W), (bias_l1[:], L1_bias), (bias_1[:], b1), (bias_2[:], b2),
                   (b3_rows[:], L3_b.partition_broadcast(P))]

        agg = pb("agg", [P, 2 * CW])
        p_gen = pb("p_gen", [P, GEN_BANKS, 512])
        p_mix = pb("p_mix", [P, CW])
        p_rows = pb("p_rows", [P, CW])
        p_turn = pb("p_turn", [P, CW])

        x_loaded = [sem(f"x_loaded{i}") for i in range(X_PARTS)]
        x_moved = sem("x_moved")
        w_loaded = sem("w_loaded")
        slot_loaded = [sem(f"slot_loaded{s}") for s in range(SLOTS)]
        kept_loaded = sem("kept_loaded")
        ident_zeroed = sem("ident_zeroed")
        ident_ready = sem("ident_ready")
        consts_ready = sem("consts_ready")
        tile_used = sem("tile_used")
        vec_tile = sem("vec_tile")
        hi_ready = sem("hi_ready")
        deg_ready = sem("deg_ready")
        deg_step = sem("deg_step")
        copies_ready = sem("copies_ready")
        mix_done = sem("mix_done")
        scaled_ready = sem("scaled_ready")
        y_half = sem("y_half")
        relu_ready = sem("relu_ready")
        y_ready = sem("y_ready")
        rows_done = sem("rows_done")
        stats_ready = sem("stats_ready")
        moments_ready = sem("moments_ready")
        var_ready = sem("var_ready")
        rstd_ready = sem("rstd_ready")
        shift_ready = sem("shift_ready")
        norm_ready = sem("norm_ready")
        turn_done = sem("turn_done")
        x_ready = sem("x_ready")
        hidden_ready = sem("hidden_ready")
        gen_done = sem("gen_done")
        zb_ready = sem("zb_ready")
        swish_ready = sem("swish_ready")
        first_lo = sem("first_lo")
        x0_hi = sem("x0_hi")
        x0_lo = sem("x0_lo")
        gen_hi = sem("gen_hi")
        gen_lo = sem("gen_lo")
        last_in = sem("last_in")
        last_z = sem("last_z")
        last_zb = sem("last_zb")
        last_act = sem("last_act")

        ENTRY_AT = 3
        DEGREE_AT = 5
        SCALE_AT = 6
        BIAS_AT = 6
        SWISH_AT = 7
        STORE_AT = 15
        RESIDUAL_AT = {0: 6, 1: 2, 3: 5, 5: 7}
        ROWS_AT = {0: 1, 1: 1, 3: 4, 5: 3}
        STATS_AT = {0: 8, 1: 5, 3: 7, 5: 8}
        MOMENTS_AT = {0: 10, 1: 7, 3: 8, 5: 10}
        SHIFT_AT = {0: 12, 1: 9, 3: 9, 5: 12}
        NORM_AT = {0: 14, 1: 11, 3: 12, 5: 14}
        TURN_AT = {0: 11, 1: 9}
        X_AT = {0: 14, 1: 14}
        EARLY = {1: 14, 2: 14, 3: 14, 4: 14, 5: 12}
        GEN_LAG = {1: 5, 2: 5, 3: 4, 4: 5, 5: 4}
        GEN_LEAD = {1: 2, 2: 2, 3: 2, 5: 5}
        GEN_HOLD = {1: 1, 2: 3, 3: 3, 4: 1, 5: 1}

        block = ctx.enter_context(nc.Block())

        def nth(passes, p, c):
            return passes.index(p) * CHUNKS + c

        def chunk_of(t, c):
            return t[:, bass.ds(c * CW, CW)]

        def bank_of(c):
            return agg[:, bass.ds((c % 2) * CW, CW)]

        def raw_tile(c, t):
            if t < STREAMED:
                return ring[:, t % SLOTS, :]
            return kept[:, bass.ds(c * KEPT + t - STREAMED, 1), :].rearrange("p o n -> p (o n)")

        def op_tile(buf, t):
            return buf[:, t * GW:(t + 1) * GW]

        def nth_hi(p, c, t):
            if p == 0:
                return len(SPLIT_FIRST) * c + SPLIT_FIRST.index(t) + 1
            return len(SPLIT_FIRST) * CHUNKS + ((p - 1) * CHUNKS + c) * TILES + t + 1

        def nth_gen(p, t):
            return GEN_PASSES.index(p) * TILES + t + 1

        def split_place(p, t):
            return SPLIT_FIRST.index(t) if p == 0 else t % SPLITS

        def wait_loaded(eng, p, c, t):
            if t < STREAMED:
                eng.wait_ge(slot_loaded[t % SLOTS], 16 * (LOADS * (p * CHUNKS + c) + t // SLOTS + 1))
            elif p == 0:
                eng.wait_ge(kept_loaded, 16 * (c + 1))

        @block.sync
        def _(sp):
            def load_chunk(p, c):
                first = isinstance(c, int) and c == 0
                for t in range(TILES if p == 0 and first else STREAMED):
                    if p == 0 and first and t % (TILES // X_PARTS) == 0:
                        i = t * X_PARTS // TILES
                        part = slice(i * N // X_PARTS, (i + 1) * N // X_PARTS)
                        sp.dma_start(hidden[:, part], x_blocks[:, part]).then_inc(x_loaded[i], 16)
                    if t >= STREAMED:
                        continue
                    before = (p * CHUNKS + c) * TILES + t + 1 - SLOTS - (KEPT if t < SLOTS else 0)
                    if not (p == 0 and first and t < SLOTS):
                        if p == 0 or (p == 1 and first and t < SLOTS):
                            sp.wait_ge(tile_used, before)
                        sp.wait_ge(vec_tile, before)
                    sp.dma_start(ring[:, t % SLOTS, :], adj_tiles[c, t]).then_inc(slot_loaded[t % SLOTS], 16)
                if p == 0:
                    if not first:
                        sp.wait_ge(kept_loaded, 16 * c)
                    sp.dma_start(kept[:, bass.ds(c * KEPT, KEPT), :],
                                 adj_tiles[c, STREAMED:TILES].rearrange("t p n -> p t n")).then_inc(kept_loaded, 16)

            for p in range(PASSES):
                load_chunk(p, 0)
                with sp.Fori(1, CHUNKS) as c:
                    load_chunk(p, c)

        @block.tensor
        def _(pe):
            def gen(p, t):
                c_of = t * BPT // BPC
                if p in (1, 2):
                    src = xT
                    pe.wait_ge(x_ready, nth(TURN_PASSES, p - 1, c_of) + 1)
                else:
                    src = hidden
                    pe.wait_ge(hidden_ready, nth(HIDDEN_PASSES, p - 1, c_of) + 1)
                if t >= GEN_BANKS:
                    pe.wait_ge(gen_lo, (p - 1) * TILES + t + 1 - GEN_BANKS)
                elif p > 1:
                    pe.wait_ge(gen_lo, (p - 1) * TILES)
                for b in range(BPT):
                    j = t * BPT + b
                    dst = p_gen[:, t % GEN_BANKS, b * D:(b + 1) * D]
                    w = {1: w_l1, 2: w_1, 3: w_2, 5: w_3}[p]
                    last = nc.tensor.matmul(dst, src[:, j * P:(j + 1) * P], w[:], start=True, stop=True)
                last.then_inc(gen_done, 1)

            def tile_whole(c, t):
                wait_loaded(pe, 0, c, t)
                raw = raw_tile(c, t)
                for b in range(BPT):
                    j = t * BPT + b
                    last = nc.tensor.matmul(bank_of(c), hidden[:, j * D:(j + 1) * D],
                                            raw[:, b * CW:(b + 1) * CW], start=(j == 0), stop=(j == NB - 1))
                last.then_inc(tile_used, 1)

            def tile_split(p, c, t):
                s = split_place(p, t)
                pe.wait_ge(hi_ready, nth_hi(p, c, t))
                for b in range(BPT):
                    j = t * BPT + b
                    a_hi = adj_hi[:, s, b * CW:(b + 1) * CW]
                    nc.tensor.matmul(bank_of(c), op_hi[:, j * D:(j + 1) * D], a_hi, start=(j == 0), stop=False)
                    nc.tensor.matmul(bank_of(c), op_lo[:, j * D:(j + 1) * D], a_hi, start=False, stop=False)
                if p == 0:
                    pe.wait_ge(first_lo, nth_hi(p, c, t))
                else:
                    pe.wait_ge(vec_tile, (p * CHUNKS + c) * TILES + t + 1)
                for b in range(BPT):
                    j = t * BPT + b
                    last = nc.tensor.matmul(bank_of(c), op_hi[:, j * D:(j + 1) * D],
                                            adj_lo[:, s, b * CW:(b + 1) * CW], start=False, stop=(j == NB - 1))
                last.then_inc(tile_used, 1)

            def post(p, c, at):
                if p == 0 and at == ROWS_AT[p]:
                    pe.wait_ge(deg_ready, c + 1)
                    pe.wait_ge(copies_ready, 2 * (c + 1))
                    for b in range(BPC):
                        blk = slice(b * P, (b + 1) * P)
                        nc.tensor.matmul(p_turn[:, b:b + 1], deg_sum[:, blk], ones[:], start=True, stop=True)
                        nc.tensor.matmul(p_mix[:, blk], t_in[:, blk], w_neigh[:], start=True, stop=True)
                        last = nc.tensor.matmul(p_rows[:, blk], t_x[:, blk], w_self[:], start=True, stop=True)
                    last.then_inc(mix_done, 1)
                if p in RELU_PASSES and at == ROWS_AT[p]:
                    pe.wait_ge(y_ready, nth(NORM_PASSES, p, c) + 1)
                    for b in range(BPC):
                        last = nc.tensor.transpose(p_rows[:, b * D:(b + 1) * D], t_y[:, b * P:(b + 1) * P], ident[:])
                    last.then_inc(rows_done, 1)
                if p in TURN_PASSES and at == TURN_AT[p]:
                    pe.wait_ge(norm_ready, BPC * (nth(NORM_PASSES, p, c) + 1))
                    for b in range(BPC):
                        last = nc.tensor.transpose(p_turn[:, b * P:(b + 1) * P], t_x[:, b * D:(b + 1) * D], ident[:])
                    last.then_inc(turn_done, 1)
                if p in HIDDEN_PASSES and at == 6:
                    pe.wait_ge(hidden_ready, nth(HIDDEN_PASSES, p, c) + 1)
                if p == LAST and at == ROWS_AT[p]:
                    pe.wait_ge(last_in, c + 1)
                    for b in range(BPC):
                        last = nc.tensor.matmul(p_mix[:, b * D:(b + 1) * D], t_in[:, b * P:(b + 1) * P], w_3[:],
                                                start=True, stop=True)
                    last.then_inc(last_z, 1)

            def chunk(p, c, posted):
                first = isinstance(c, int) and c == 0
                final = isinstance(c, int) and c == CHUNKS - 1
                for t in range(TILES):
                    if p == 0:
                        if first and t % (TILES // X_PARTS) == 0:
                            pe.wait_ge(x_loaded[t * X_PARTS // TILES], 16)
                        if t in SPLIT_FIRST:
                            if first:
                                pe.wait_ge(x0_lo, SPLIT_FIRST.index(t) + 1)
                            tile_split(p, c, t)
                        else:
                            tile_whole(c, t)
                    else:
                        if first and (t == 0 or t >= EARLY[p]):
                            ready = max(EARLY[p], t + 1)
                            pe.wait_ge(gen_lo, (p - 1) * TILES + ready)
                        tile_split(p, c, t)
                    if posted:
                        post(*posted, t)
                    if p in GEN_PASSES and first and EARLY[p] <= t + GEN_LEAD[p] < TILES:
                        gen(p, t + GEN_LEAD[p])
                    if p + 1 in GEN_PASSES and final and t < EARLY[p + 1]:
                        gen(p + 1, t)

            for p in range(PASSES):
                chunk(p, 0, (p - 1, CHUNKS - 1) if p else None)
                if p == 0:
                    pe.wait_ge(ident_ready, 1)
                    pe.wait_ge(consts_ready, 2)
                    pe.wait_ge(w_loaded, 16 * len(WEIGHTS))
                with pe.Fori(1, CHUNKS - 1) as c:
                    chunk(p, c, (p, c - 1))
                chunk(p, CHUNKS - 1, (p, CHUNKS - 2))
            for t in range(TILES):
                post(LAST, CHUNKS - 1, t)

        @block.scalar
        def _(act):
            def load_xt(c):
                act.dma_start(chunk_of(xT, c), x_t[:, bass.ds(c * CW, CW)]).then_inc(x_moved, 16)

            def gen(p, t):
                value = p_gen[:, t % GEN_BANKS, 0:GW]
                if p == LAST:
                    half = slice(t % 2 * GW, (t % 2 + 1) * GW)
                    act.wait_ge(zb_ready, t + 1)
                    nc.scalar.activation(t_act[:, half], t_y[:, half], ACT.Silu).then_inc(swish_ready, 1)
                    act.wait_ge(swish_ready, t + 1)
                    value = t_act[:, half]
                elif p == 4:
                    act.wait_ge(norm_ready, BPC * (nth(NORM_PASSES, 3, t * BPT // BPC) + 1))
                    act.wait_ge(tile_used, (p * CHUNKS - 1) * TILES + t + 1)
                    value = op_tile(xT, t)
                else:
                    act.wait_ge(gen_done, nth_gen(p, t))
                nc.scalar.copy(op_tile(op_hi, t), value).then_inc(gen_hi, 1)

            def hi_tile(p, c, t):
                wait_loaded(act, p, c, t)
                if p > 0:
                    act.wait_ge(tile_used, (p * CHUNKS + c) * TILES + t + 1 - SPLITS)
                elif not (isinstance(c, int) and c == 0):
                    act.wait_ge(tile_used, (c - 1) * TILES + t + 1)
                nc.scalar.copy(adj_hi[:, split_place(p, t), :], raw_tile(c, t)).then_inc(hi_ready, 1)

            def post(p, c, at):
                chunk_ended = (p * CHUNKS + c + 1) * TILES
                if p == 0 and at == ENTRY_AT:
                    act.wait_ge(x_moved, 16 * (c + 1))
                    act.nop(nofuse=True)
                    nc.scalar.copy(t_x[:], chunk_of(xT, c)).then_inc(copies_ready, 1)
                    act.wait_ge(tile_used, chunk_ended)
                    nc.scalar.copy(t_in[:], bank_of(c)).then_inc(copies_ready, 1)
                if p == 0 and at == SCALE_AT:
                    act.wait_ge(deg_step, 2 * (c + 1))
                    for b in range(BPC):
                        nc.scalar.activation(t_act[:, b * D:(b + 1) * D], p_mix[:, b * D:(b + 1) * D], ACT.Copy,
                                             scale=rdeg[:, b:b + 1]).then_inc(scaled_ready, 1)
                if p in RELU_PASSES and at == ENTRY_AT:
                    act.wait_ge(tile_used, chunk_ended)
                    bias = {1: bias_l1, 3: bias_2}[p]
                    nc.scalar.activation(t_in[:], bank_of(c), ACT.Relu, bias=bias[:]).then_inc(relu_ready, 1)
                if p in NORM_PASSES and at == NORM_AT[p]:
                    act.wait_ge(shift_ready, nth(NORM_PASSES, p, c) + 1)
                    rows = p_rows if p in RELU_PASSES else t_y
                    if p == LAST:
                        act.wait_ge(x_moved, 16 * (CHUNKS + c))
                    for b in range(BPC):
                        dst = xT[:, bass.ds(c * CW + b * D, D)] if p == 3 else t_x[:, b * D:(b + 1) * D]
                        nc.scalar.activation(dst, rows[:, b * D:(b + 1) * D], ACT.Identity,
                                             bias=shift[:, b:b + 1], scale=rstd[:, b:b + 1]).then_inc(norm_ready, 1)
                if p in TURN_PASSES and at == X_AT[p]:
                    act.wait_ge(turn_done, nth(TURN_PASSES, p, c) + 1)
                    act.nop(nofuse=True)
                    nc.scalar.copy(chunk_of(xT, c), p_turn[:]).then_inc(x_ready, 1)
                if p in HIDDEN_PASSES and at == ENTRY_AT:
                    act.wait_ge(tile_used, chunk_ended)
                    if p == 2:
                        nc.scalar.activation(chunk_of(hidden, c), bank_of(c), ACT.Relu,
                                             bias=bias_1[:]).then_inc(hidden_ready, 1)
                    else:
                        nc.scalar.copy(chunk_of(hidden, c), bank_of(c)).then_inc(hidden_ready, 1)
                if p == LAST:
                    if at == ENTRY_AT:
                        act.wait_ge(tile_used, chunk_ended)
                        nc.scalar.copy(t_in[:], bank_of(c)).then_inc(last_in, 1)
                    if at == SWISH_AT:
                        act.wait_ge(last_zb, c + 1)
                        nc.scalar.activation(t_act[:], t_y[:], ACT.Silu).then_inc(last_act, 1)
                    if at == STORE_AT:
                        act.wait_ge(norm_ready, BPC * (nth(NORM_PASSES, p, c) + 1))
                        act.dma_start(out[bass.ds(c * CW, CW), :].rearrange("(b p) d -> p b d", p=P),
                                      t_x[:].rearrange("p (b d) -> p b d", b=BPC)).then_inc(x_moved, 16)

            def chunk(p, c, posted):
                first = isinstance(c, int) and c == 0
                final = isinstance(c, int) and c == CHUNKS - 1
                for t in range(TILES + max(GEN_LAG.values())):
                    if p < LAST and final and 0 <= t - GEN_LAG[p + 1] < EARLY[p + 1]:
                        gen(p + 1, t - GEN_LAG[p + 1])
                    if p > 0 and first and EARLY[p] <= t - GEN_HOLD[p] < TILES:
                        gen(p, t - GEN_HOLD[p])
                    if posted and t < TILES:
                        post(*posted, t)
                    if p == 0 and first and t == ENTRY_AT + 1:
                        for dst, src in WEIGHTS:
                            act.dma_start(dst, src).then_inc(w_loaded, 16)
                    if p == 0 and t == ENTRY_AT + 1:
                        load_xt(c)
                    if p == 0 and first and t in SPLIT_FIRST:
                        act.wait_ge(x_loaded[t * X_PARTS // TILES], 16)
                        nc.scalar.copy(op_tile(op_hi, t), op_tile(hidden, t)).then_inc(x0_hi, 1)
                    if t < TILES and (p > 0 or t in SPLIT_FIRST):
                        hi_tile(p, c, t)

            for p in range(PASSES):
                chunk(p, 0, (p - 1, CHUNKS - 1) if p else None)
                if p == 0:
                    act.wait_ge(w_loaded, 16 * len(WEIGHTS))
                with act.Fori(1, CHUNKS - 1) as c:
                    chunk(p, c, (p, c - 1))
                chunk(p, CHUNKS - 1, (p, CHUNKS - 2))
            for t in range(TILES):
                post(LAST, CHUNKS - 1, t)
            act.wait_ge(x_moved, 16 * 2 * CHUNKS)

        @block.vector
        def _(dve):
            def gen_bias(t):
                half = slice(t % 2 * GW, (t % 2 + 1) * GW)
                dve.wait_ge(gen_done, nth_gen(LAST, t))
                nc.vector.tensor_tensor(t_y[:, half].rearrange("p (b d) -> p b d", b=BPT),
                                        p_gen[:, t % GEN_BANKS, 0:GW].rearrange("p (b d) -> p b d", b=BPT),
                                        b3_rows[:].unsqueeze(1).broadcast_to([P, BPT, D]),
                                        ALU.add).then_inc(zb_ready, 1)

            def gen(p, t):
                dve.wait_ge(gen_hi, (p - 1) * TILES + t + 1)
                if p == LAST:
                    value = t_act[:, t % 2 * GW:(t % 2 + 1) * GW]
                elif p == 4:
                    value = op_tile(xT, t)
                else:
                    value = p_gen[:, t % GEN_BANKS, 0:GW]
                nc.vector.tensor_tensor(op_tile(op_lo, t), value, op_tile(op_hi, t).bitcast(fp32),
                                        ALU.subtract).then_inc(gen_lo, 1)

            def degree_tile(c, t):
                wait_loaded(dve, 0, c, t)
                if t == 0:
                    if not (isinstance(c, int) and c == 0):
                        dve.wait_ge(deg_ready, c)
                    nc.vector.tensor_copy(deg_part[:], raw_tile(c, t)).then_inc(vec_tile, 1)
                else:
                    dve.wait_ge(vec_tile, c * TILES + t)
                    nc.vector.tensor_tensor(deg_part[:], deg_part[:], raw_tile(c, t), ALU.add).then_inc(vec_tile, 1)

            def lo_tile(p, c, t):
                s = split_place(p, t)
                dve.wait_ge(hi_ready, nth_hi(p, c, t))
                nc.vector.tensor_tensor(adj_lo[:, s, :], raw_tile(c, t), adj_hi[:, s, :].bitcast(fp32),
                                        ALU.subtract).then_inc(vec_tile if p else first_lo, 1)

            def post(p, c, at):
                if p == 0 and at == DEGREE_AT:
                    dve.wait_ge(mix_done, c + 1)
                    nc.vector.tensor_scalar(rdeg[:], p_turn[:, 0:BPC], 1.0, None, ALU.max).then_inc(deg_step, 1)
                    dve.wait_ge(deg_step, 2 * c + 1)
                    nc.vector.reciprocal(rdeg[:], rdeg[:]).then_inc(deg_step, 1)
                if p == 0 and at == RESIDUAL_AT[p]:
                    dve.wait_ge(scaled_ready, BPC * (c + 1))
                    nc.vector.tensor_tensor(t_y[:], t_act[:], p_rows[:], ALU.add).then_inc(y_half, 1)
                    dve.wait_ge(y_half, c + 1)
                    nc.vector.tensor_tensor(t_y[:], t_y[:], chunk_of(hidden, c), ALU.add).then_inc(y_ready, 1)
                if p in RELU_PASSES and at == RESIDUAL_AT[p]:
                    dve.wait_ge(relu_ready, nth(RELU_PASSES, p, c) + 1)
                    nc.vector.tensor_tensor(t_y[:], t_in[:], chunk_of(xT, c), ALU.add).then_inc(y_ready, 1)
                if p in NORM_PASSES and at == STATS_AT[p]:
                    n = nth(NORM_PASSES, p, c)
                    rows = p_rows if p in RELU_PASSES else t_y
                    if p in RELU_PASSES:
                        dve.wait_ge(rows_done, nth(RELU_PASSES, p, c) + 1)
                    else:
                        dve.wait_ge(y_ready, n + 1)
                    for b in range(BPC):
                        nc.vector.bn_stats(stats[:, b, :], rows[:, b * D:(b + 1) * D]).then_inc(stats_ready, 1)
                if p in NORM_PASSES and at == MOMENTS_AT[p]:
                    dve.wait_ge(stats_ready, BPC * (nth(NORM_PASSES, p, c) + 1))
                    dve.nop(nofuse=True)
                    for b in range(BPC):
                        nc.vector.bn_aggr(moments[:, b, :], stats[:, b, :]).then_inc(moments_ready, 1)
                if p in NORM_PASSES and at == SHIFT_AT[p]:
                    dve.wait_ge(rstd_ready, nth(NORM_PASSES, p, c) + 1)
                    nc.vector.scalar_tensor_tensor(out=shift[:], in0=moments[:, :, 0], scalar=-1.0, in1=rstd[:],
                                                   op0=ALU.mult, op1=ALU.mult).then_inc(shift_ready, 1)
                if p == LAST and at == BIAS_AT:
                    dve.wait_ge(last_z, c + 1)
                    nc.vector.tensor_tensor(t_y[:].rearrange("p (b d) -> p b d", b=BPC),
                                            p_mix[:].rearrange("p (b d) -> p b d", b=BPC),
                                            b3_rows[:].unsqueeze(1).broadcast_to([P, BPC, D]),
                                            ALU.add).then_inc(last_zb, 1)
                if p == LAST and at == RESIDUAL_AT[p]:
                    dve.wait_ge(last_act, c + 1)
                    nc.vector.tensor_tensor(t_y[:], t_act[:], chunk_of(xT, c),
                                            ALU.add).then_inc(y_ready, 1)

            def chunk(p, c, posted):
                first = isinstance(c, int) and c == 0
                final = isinstance(c, int) and c == CHUNKS - 1
                for t in range(TILES + max(GEN_LAG.values())):
                    if p == LAST - 1 and final and 0 <= t - GEN_LAG[LAST] + 1 < EARLY[LAST]:
                        gen_bias(t - GEN_LAG[LAST] + 1)
                    if p < LAST and final and 0 <= t - GEN_LAG[p + 1] < EARLY[p + 1]:
                        gen(p + 1, t - GEN_LAG[p + 1])
                    if p == LAST and first and EARLY[LAST] <= t - GEN_HOLD[LAST] + 1 < TILES:
                        gen_bias(t - GEN_HOLD[LAST] + 1)
                    if p > 0 and first and EARLY[p] <= t - GEN_HOLD[p] < TILES:
                        gen(p, t - GEN_HOLD[p])
                    if posted and t < TILES:
                        post(*posted, t)
                    if p == 0 and first and t in SPLIT_FIRST:
                        dve.wait_ge(x0_hi, SPLIT_FIRST.index(t) + 1)
                        nc.vector.tensor_tensor(op_tile(op_lo, t), op_tile(hidden, t), op_tile(op_hi, t).bitcast(fp32),
                                                ALU.subtract).then_inc(x0_lo, 1)
                    if p == 0 and t < TILES:
                        if t in SPLIT_FIRST:
                            lo_tile(p, c, t)
                        degree_tile(c, t)
                    elif t < TILES:
                        lo_tile(p, c, t)
                    if p == 0 and t == TILES - 1:
                        dve.wait_ge(vec_tile, (c + 1) * TILES)
                        nc.vector.tensor_tensor(deg_sum[:], deg_part[:, 0:CW], deg_part[:, CW:2 * CW],
                                                ALU.add).then_inc(deg_ready, 1)

            for p in range(PASSES):
                chunk(p, 0, (p - 1, CHUNKS - 1) if p else None)
                if p == 0:
                    dve.wait_ge(w_loaded, 16 * len(WEIGHTS))
                with dve.Fori(1, CHUNKS - 1) as c:
                    chunk(p, c, (p, c - 1))
                chunk(p, CHUNKS - 1, (p, CHUNKS - 2))
            for t in range(TILES):
                post(LAST, CHUNKS - 1, t)

        @block.gpsimd
        def _(pool):
            nc.gpsimd.memset(ident[:], 0.0).then_inc(ident_zeroed, 1)
            pool.wait_ge(ident_zeroed, 1)
            nc.gpsimd.affine_select(out=ident[:], in_=ident[:], compare_op=ALU.not_equal, fill=1.0, base=0,
                                    pattern=[[-1, P]], channel_multiplier=1).then_inc(ident_ready, 1)
            nc.gpsimd.memset(ones[:], 1.0).then_inc(consts_ready, 1)
            nc.gpsimd.memset(minus_half[:], -0.5).then_inc(consts_ready, 1)
            pool.wait_ge(consts_ready, 2)
            with pool.Fori(0, len(NORM_PASSES) * CHUNKS) as n:
                pool.wait_ge(moments_ready, BPC * (n + 1))
                pool.nop(nofuse=True)
                nc.gpsimd.tensor_scalar(var_eps[:], moments[:, :, 1], EPS, None, ALU.add).then_inc(var_ready, 1)
                pool.wait_ge(var_ready, n + 1)
                nc.gpsimd.tensor_tensor(rstd[:], var_eps[:], minus_half[:], ALU.pow).then_inc(rstd_ready, 1)


def kernel(x, adj, L0_gnn_W_self, L0_gnn_W_neigh, L1_gnn_kernel, L1_gnn_bias, L2_gnn_W1, L2_gnn_b1, L2_gnn_W2,
           L2_gnn_b2, L3_gnn_W, L3_gnn_b):
    import numpy as _np
    import concourse.bacc as _bacc
    from concourse import mybir as _mybir
    from concourse.bass_utils import run_bass_kernel_spmd as _run

    P, CW, BPT = 128, 512, 2
    x, adj = _np.asarray(x), _np.asarray(adj)
    n, d = x.shape
    tiles = adj.T.reshape(n // (BPT * P), BPT, P, n // CW, CW).transpose(3, 0, 2, 1, 4)
    arrays = {
        "adj_tiles": tiles.reshape(n // CW, n // (BPT * P), P, BPT * CW),
        "x_blocks": x.reshape(n // P, P, d).transpose(1, 0, 2).reshape(P, n * d // P),
        "x_t": x.T,
        "W_self": L0_gnn_W_self, "W_neigh": L0_gnn_W_neigh, "L1_kernel": L1_gnn_kernel,
        "L1_bias": _np.asarray(L1_gnn_bias).reshape(d, 1), "W1": L2_gnn_W1,
        "b1": _np.asarray(L2_gnn_b1).reshape(d, 1), "W2": L2_gnn_W2, "b2": _np.asarray(L2_gnn_b2).reshape(d, 1),
        "L3_W": L3_gnn_W, "L3_b": _np.asarray(L3_gnn_b),
    }
    arrays = {name: _np.ascontiguousarray(a) for name, a in arrays.items()}
    nc = _bacc.Bacc("TRN2", target_bir_lowering=False, num_devices=1)
    args = [nc.dram_tensor(name, a.shape, _mybir.dt.from_np(a.dtype), kind="ExternalInput").ap()
            for name, a in arrays.items()]
    args.append(nc.dram_tensor("out", (n, d), _mybir.dt.float32, kind="ExternalOutput").ap())
    bass_gnn_residual_norm_kernel(nc, *args)
    r = _run(nc, [arrays], core_ids=[0])
    return r.results[0]["out"]
```
